# Optimizing a Trainium2 kernel written in Bass

```python
import numpy as np
import jax
import jax.numpy as jnp

def _softmax(x, axis=-1):
    return jax.nn.softmax(x, axis=axis)

def _gelu(x):
    return jax.nn.gelu(x, approximate=True)

def _silu(x):
    return jax.nn.silu(x)

def _sigmoid(x):
    return jax.nn.sigmoid(x)

def _layernorm(x, axis=-1, eps=1e-05):
    m = jnp.mean(x, axis=axis, keepdims=True)
    v = jnp.var(x, axis=axis, keepdims=True)
    return (x - m) / jnp.sqrt(v + eps)

def _scatter_add(tgt, idx, src, axis=0):
    return tgt.at[idx].add(src)

def _segment_sum(src, seg, n):
    return jax.ops.segment_sum(src, seg, n)
kernel_name = 'mk_adj_preln_d2_adj_r2_819f32'

def setup_inputs(seed: int=0):
    np.random.seed(seed)
    _w = jnp.asarray

    def _rec_inputs():
        import jax
        import jax.numpy as jnp
        _gk = jax.random.key(seed)
        x = -0.0005207 + 1.001 * jax.random.normal(jax.random.fold_in(_gk, 1), (3327, 256), jnp.float32)
        _w = (1.0 + jnp.arange(3327, dtype=jnp.float32)) ** (-0.5)
        _w = _w / _w.mean()
        _pij = jnp.clip(0.00961827 * _w[:, None] * _w[None, :], 0.0, 1.0)
        _a = jax.random.uniform(jax.random.fold_in(_gk, 2), (3327, 3327)) < _pij
        _a = jnp.logical_or(_a, jnp.eye(3327, dtype=bool))
        _af = _a.astype(jnp.float32)
        _af = _af * jax.random.uniform(jax.random.fold_in(_gk, 3), (3327, 3327), jnp.float32, 0.05, 1)
        adj = _af
        return (x, adj)
    x, adj = _rec_inputs()

    def _L0_gnn_setup():
        import jax, jax.numpy as jnp
        import numpy as np
        N, D_IN, D_ATTN, STEPS, P_NUC, TAU = (2048, 256, 64, 2, 0.9, 1.0)
        LN_EPS = 1e-05

        def _xavier(key, shape):
            fan_in, fan_out = (shape[-2], shape[-1])
            lim = np.sqrt(6.0 / (fan_in + fan_out))
            return jax.random.uniform(key, shape, jnp.float32, -lim, lim)

        def _adj_from_feats(Xa, W1, W2, W3):
            Q = Xa @ W1
            K = Xa @ W3
            logits = Q @ W2 @ K.T / TAU
            idx = jnp.argsort(-logits, axis=1)
            vals = jnp.take_along_axis(logits, idx, axis=1)
            csum = jnp.cumsum(jax.nn.softmax(vals, axis=1), axis=1)
            k_i = jnp.sum(csum < P_NUC, axis=1) + 1
            ranks = jnp.arange(logits.shape[1])[None, :]
            keep_sorted = ranks < k_i[:, None]
            inv = jnp.argsort(idx, axis=1)
            keep = jnp.take_along_axis(keep_sorted, inv, axis=1)
            masked = jnp.where(keep, logits, -jnp.inf)
            return jax.nn.softmax(masked, axis=1)
        key = jax.random.key(seed)
        ks = jax.random.split(key, 9)
        return {'X': jax.random.normal(ks[0], (N, D_IN), jnp.float32), 'S': jax.random.uniform(ks[1], (N, N), jnp.float32), 'W1': _xavier(ks[2], (D_IN, D_ATTN)), 'W2': _xavier(ks[3], (D_ATTN, D_ATTN)), 'W3': _xavier(ks[4], (D_IN, D_ATTN)), 'U1': _xavier(ks[5], (STEPS, D_IN, D_IN)), 'U2': _xavier(ks[6], (STEPS, D_IN, D_IN)), 'U3': _xavier(ks[7], (STEPS, D_IN, D_IN)), 'gamma': jnp.ones((D_IN,), jnp.float32), 'beta': jnp.zeros((D_IN,), jnp.float32)}
    _L0_gnn_all = _L0_gnn_setup()
    _L0_gnn_in = {k: v for k, v in _L0_gnn_all.items() if k in ('W1', 'W2', 'W3', 'U1', 'U2', 'U3', 'gamma', 'beta')}
    del _L0_gnn_all

    def _L1_gnn_setup():
        import jax, jax.numpy as jnp
        import numpy as np
        N = 4096
        D_IN = 256
        D_OUT = 256
        NEG_BIG = -9000000000000000.0
        key = jax.random.key(seed)
        kx, ka, kw, kb, kn, ke = jax.random.split(key, 6)
        x = jax.random.normal(kx, (N, D_IN), dtype=jnp.float32)
        adj = (jax.random.uniform(ka, (N, N)) > 0.9).astype(jnp.float32)
        stdv = 1.0 / np.sqrt(D_OUT)
        weight = jax.random.uniform(kw, (D_IN, D_OUT), minval=-stdv, maxval=stdv, dtype=jnp.float32)
        bias = jax.random.uniform(kb, (D_OUT,), minval=-stdv, maxval=stdv, dtype=jnp.float32)
        node_w = jax.random.uniform(kn, (D_IN, 1), minval=-1.0, maxval=1.0, dtype=jnp.float32)
        stdv_e = 1.0 / np.sqrt(D_IN)
        edge_w = jax.random.uniform(ke, (D_IN, D_IN), minval=-stdv_e, maxval=stdv_e, dtype=jnp.float32)
        return {'x': x, 'adj': adj, 'weight': weight, 'bias': bias, 'node_w': node_w, 'edge_w': edge_w}
    _L1_gnn_all = _L1_gnn_setup()
    _L1_gnn_in = {k: v for k, v in _L1_gnn_all.items() if k in ('weight', 'bias', 'node_w', 'edge_w')}
    del _L1_gnn_all
    return {'x': x, 'adj': adj, 'L0_gnn_W1': _L0_gnn_in['W1'], 'L0_gnn_W2': _L0_gnn_in['W2'], 'L0_gnn_W3': _L0_gnn_in['W3'], 'L0_gnn_U1': _L0_gnn_in['U1'], 'L0_gnn_U2': _L0_gnn_in['U2'], 'L0_gnn_U3': _L0_gnn_in['U3'], 'L0_gnn_gamma': _L0_gnn_in['gamma'], 'L0_gnn_beta': _L0_gnn_in['beta'], 'L1_gnn_weight': _L1_gnn_in['weight'], 'L1_gnn_bias': _L1_gnn_in['bias'], 'L1_gnn_node_w': _L1_gnn_in['node_w'], 'L1_gnn_edge_w': _L1_gnn_in['edge_w']}

def reference(x, adj, L0_gnn_W1, L0_gnn_W2, L0_gnn_W3, L0_gnn_U1, L0_gnn_U2, L0_gnn_U3, L0_gnn_gamma, L0_gnn_beta, L1_gnn_weight, L1_gnn_bias, L1_gnn_node_w, L1_gnn_edge_w):
    import jax
    import jax.numpy as jnp

    def _L0_gnn_ref(X, S, W1, W2, W3, U1, U2, U3, gamma, beta):
        import jax, jax.numpy as jnp
        import numpy as np
        N, D_IN, D_ATTN, STEPS, P_NUC, TAU = (2048, 256, 64, 2, 0.9, 1.0)
        LN_EPS = 1e-05

        def _xavier(key, shape):
            fan_in, fan_out = (shape[-2], shape[-1])
            lim = np.sqrt(6.0 / (fan_in + fan_out))
            return jax.random.uniform(key, shape, jnp.float32, -lim, lim)

        def _adj_from_feats(Xa, W1, W2, W3):
            Q = Xa @ W1
            K = Xa @ W3
            logits = Q @ W2 @ K.T / TAU
            idx = jnp.argsort(-logits, axis=1)
            vals = jnp.take_along_axis(logits, idx, axis=1)
            csum = jnp.cumsum(jax.nn.softmax(vals, axis=1), axis=1)
            k_i = jnp.sum(csum < P_NUC, axis=1) + 1
            ranks = jnp.arange(logits.shape[1])[None, :]
            keep_sorted = ranks < k_i[:, None]
            inv = jnp.argsort(idx, axis=1)
            keep = jnp.take_along_axis(keep_sorted, inv, axis=1)
            masked = jnp.where(keep, logits, -jnp.inf)
            return jax.nn.softmax(masked, axis=1)
        n = X.shape[0]
        S = S + jnp.eye(n, dtype=X.dtype)
        Rf = S / jnp.clip(S.sum(axis=1, keepdims=True), 1e-12)
        Rb = S / jnp.clip(S.sum(axis=0), 1e-12)[:, None]
        Xf, Xb, Xa = (X, X, X)
        Z = jnp.zeros_like(X)
        for s in range(STEPS):
            A = _adj_from_feats(Xa, W1, W2, W3)
            Xf = Rf @ Xf
            Xb = Rb @ Xb
            Xa = A @ Xa
            Z = Z + (Xf @ U1[s] + Xb @ U2[s] + Xa @ U3[s])
        Y = X + Z
        mu = Y.mean(axis=-1, keepdims=True)
        var = Y.var(axis=-1, keepdims=True)
        return (Y - mu) / jnp.sqrt(var + LN_EPS) * gamma + beta

    def _L1_gnn_ref(x, adj, weight, bias, node_w, edge_w):
        import jax, jax.numpy as jnp
        import numpy as np
        N = 4096
        D_IN = 256
        D_OUT = 256
        NEG_BIG = -9000000000000000.0
        node_att = jax.nn.softmax(x @ node_w, axis=0)
        h = x @ edge_w
        e = h @ h.T
        e = jnp.where(adj > 0, e, NEG_BIG)
        edge_att = jax.nn.softmax(e, axis=1)
        combined_att = node_att * edge_att
        support = x @ weight
        output = adj * combined_att @ support
        return output + bias
    h = jnp.maximum(_layernorm(x, axis=-1), 0.0)
    x = x + _L0_gnn_ref(h, adj, L0_gnn_W1, L0_gnn_W2, L0_gnn_W3, L0_gnn_U1, L0_gnn_U2, L0_gnn_U3, L0_gnn_gamma, L0_gnn_beta)
    h = jnp.maximum(_layernorm(x, axis=-1), 0.0)
    x = x + _L1_gnn_ref(h, adj, L1_gnn_weight, L1_gnn_bias, L1_gnn_node_w, L1_gnn_edge_w)
    return x

_drawn_inputs = setup_inputs


def setup_inputs(seed=0):
    import zlib

    import numpy as np

    out = dict(_drawn_inputs(seed))
    spreads = {'L0_gnn_gamma': (1.0, 0.2), 'L0_gnn_beta': (0.0, 0.1)}
    factors = {'L1_gnn_weight': 55.182, 'L1_gnn_bias': 2.785, 'L1_gnn_node_w': 55.538}
    for name, (base, spread) in spreads.items():
        noise = np.random.default_rng([zlib.crc32(name.encode()), seed]).standard_normal(out[name].shape)
        drawn = base * np.exp(spread * noise) if base else spread * noise
        out[name] = jnp.asarray(drawn.astype(out[name].dtype))
    for name, factor in factors.items():
        out[name] = (out[name] * factor).astype(out[name].dtype)
    return out
```

```python
from contextlib import ExitStack

import numpy as np

import concourse.bass as bass
from concourse import mybir

ALU = mybir.AluOpType
ACT = mybir.ActivationFunctionType
F32 = mybir.dt.float32
F16 = mybir.dt.float16
BF16 = mybir.dt.bfloat16
AX = mybir.AxisListType

P = 128
N = 3327
NT = -(-N // P)
NPAD = NT * P
D = 256
DA = 64
KC = D // P
HALF = NT // 2
CH = 512
NCH = -(-N // CH)
NPAIR = NT // 2
GRP = 4
NGRP = -(-NT // GRP)
EPS = 1e-5
P_NUC = 0.9
LN_PSCALE = 10 * float(np.log(2.0))
NEG_BIG = -9000000000000000.0
BISECT = 19
LOG_STEP = 8.0
LEAST = 0.9 * (1 - P_NUC) / N
HROW = 2 * D + 2


class Own:

    def __init__(self, eng, sem):
        self.eng, self.sem, self.base, self.n = eng, sem, 0, 0

    def start(self, base):
        self.base, self.n = base, 0

    def link(self, ins):
        self.n += 1
        ins.then_inc(self.sem, 1)
        self.eng.wait_ge(self.sem, self.base + self.n)


def chunk_width(c):
    return min(CH, N - c * CH)


def group_blocks(q):
    return range(GRP * q, min(GRP * q + GRP, NT))


def program(nc, x, adjT, adjR, W1T, W2, W3, U1, U2, U3, gamma, beta, weight, bias, node_w, edge_w, ident_in, out):
    with ExitStack() as ctx:
        def scratch(name, shape):
            return nc.dram_tensor(name, shape, F32, kind="Internal").ap()

        h_d = scratch("h_d", (NT, P, D))
        sx_d = [scratch(f"sx{s}_d", (NT, P, D * (s + 1))) for s in range(2)]
        xa_d = [scratch(f"xa{s}_d", (NT, P, D)) for s in range(2)]
        z_d = scratch("z_d", (NT, P, D))
        x1_d = scratch("x1_d", (P, NT, D))

        psum = [ctx.enter_context(nc.psum_tensor(f"bank{b}", [P, CH], F32)) for b in range(8)]
        psL, psT, psA, psS = psum[0:2], psum[2:4], psum[4:6], psum[6:8]

        def sb_in(stack):
            return lambda name, shape, dt: stack.enter_context(nc.sbuf_tensor(name, shape, dt))

        def sem(name):
            return ctx.enter_context(nc.semaphore(name))

        sb = sb_in(ctx)
        ident = sb("ident", [P, P], F32)
        identh = sb("identh", [P, P], F16)
        rinv = sb("rinv", [P, NT], F32)
        cinv = sb("cinv", [P, NT], F32)
        rsum = sb("rsum", [P, NT], F32)
        csum = sb("csum", [P, NT], F32)

        def spread(stat):
            return stat.unsqueeze(2).to_broadcast([P, NT, D])

        def normalize(own, act_in, act_out, v, sq, mean, var, root, inv, tmp):
            own.link(nc.vector.tensor_reduce(mean[:], v[:], AX.X, ALU.add))
            own.link(nc.vector.tensor_scalar(mean[:], mean[:], 1.0 / D, None, ALU.mult))
            nc.vector.tensor_tensor(v[:], v[:], spread(mean[:]), ALU.subtract).then_inc(act_in, 1)
            own.eng.wait_ge(act_in, 1)
            own.eng.wait_ge(act_out, 1)
            own.link(nc.vector.tensor_reduce(var[:], sq[:], AX.X, ALU.add))
            nc.vector.tensor_scalar(var[:], var[:], 1.0 / D, EPS, ALU.mult, ALU.add).then_inc(act_in, 1)
            own.eng.wait_ge(act_in, 2)
            own.eng.wait_ge(act_out, 2)
            own.link(nc.vector.reciprocal(inv[:], root[:]))
            own.link(nc.vector.tensor_tensor(tmp[:], inv[:], inv[:], ALU.mult))
            own.link(nc.vector.tensor_tensor(tmp[:], tmp[:], var[:], ALU.mult))
            own.link(nc.vector.tensor_scalar(tmp[:], tmp[:], -0.5, 1.5, ALU.mult, ALU.add))
            own.link(nc.vector.tensor_tensor(inv[:], inv[:], tmp[:], ALU.mult))
            own.link(nc.vector.tensor_tensor(v[:], v[:], spread(inv[:]), ALU.mult))

        def square_and_root(act, act_in, act_out, v, sq, var, root):
            act.wait_ge(act_in, 1)
            nc.scalar.activation(sq[:], v[:], ACT.Square).then_inc(act_out, 1)
            act.wait_ge(act_in, 2)
            nc.scalar.activation(root[:], var[:], ACT.Sqrt).then_inc(act_out, 1)

        with ExitStack() as l0:
            sb0 = sb_in(l0)
            qs = sb0("qs", [P, NPAD], F16)
            kh2 = sb0("kh2", [P, NPAD], F16)
            kl2 = sb0("kl2", [P, NPAD], F16)
            wq2 = sb0("wq2", [P, KC, P], F32)
            wk2 = sb0("wk2", [P, KC, P], F32)

            with ExitStack() as s0:
                sbs = sb_in(s0)
                hb = sbs("hb", [P, NT, HROW], F16)
                phase_h(nc, sem, psum, sb_in, locals())
                layer_step(nc, sem, psL, psT, psA, psS, sb_in, 0, qs, kh2, kl2, adjT, identh, ident,
                           lambda j: hb[:, j, 0:D], lambda j: hb[:, j, D + 2:HROW],
                           lambda j: hb[:, j, 0:D + 1], lambda j: hb[:, j, D + 2:HROW],
                           sx_d[0], xa_d[0], rsum, csum)
            with ExitStack() as s1:
                sbs = sb_in(s1)
                x2h = sbs("x2h", [P, NT, 2 * D], F16)
                x2l = sbs("x2l", [P, NT, 2 * D], F16)
                xab = sbs("xab", [P, NT, 2 * D], F16)
                phase_between(nc, sem, psum, sb_in, locals())
                layer_step(nc, sem, psL, psT, psA, psS, sb_in, 1, qs, kh2, kl2, adjT, identh, ident,
                           lambda j: xab[:, j, 0:D], lambda j: xab[:, j, D:2 * D],
                           lambda j: x2h[:, j, :], lambda j: x2l[:, j, :],
                           sx_d[1], xa_d[1], rsum, csum)

        with ExitStack() as l1:
            sb1 = sb_in(l1)
            hth = sb1("hth", [P, KC, NPAD], F16)
            htl = sb1("htl", [P, KC, NPAD], F16)
            sup = sb1("sup", [P, NT, 2 * D], F16)
            natt = sb1("natt", [P, NT], F32)
            phase_mid(nc, sem, psum, sb_in, locals())
            phase_edges(nc, sem, psum, sb_in, locals())


def phase_h(nc, sem, psum, sb_in, env):
    x, W1T, W2, W3, ident_in = env["x"], env["W1T"], env["W2"], env["W3"], env["ident_in"]
    ident, identh, hb, h_d = env["ident"], env["identh"], env["hb"], env["h_d"]
    qs, kh2, kl2, wq2, wk2 = (env[n] for n in ("qs", "kh2", "kl2", "wq2", "wk2"))
    with ExitStack() as c:
        sb = sb_in(c)
        xs = sb("xs", [P, NT, D], F32)
        hrow = sb("hrow", [P, 2, D], F32)
        xT = sb("xT", [P, 2, KC, P], F32)
        q16 = sb("q16", [P, 2, P], F16)
        w1t = sb("w1t", [DA, D], F32)
        w2 = sb("w2", [DA, DA], F32)
        sq = sb("sq", [P, NT, D], F32)
        mean, var, root, inv, tmp = (sb(n, [P, NT], F32) for n in ("mean0", "var0", "root0", "inv0", "tmp0"))
        loaded, consts, own_dve = sem("h_loaded"), sem("h_consts"), sem("h_own_dve")
        var_ready, root_ready = sem("h_var_ready"), sem("h_root_ready")
        h_ready, h_stored = sem("h_ready"), sem("h_stored")
        w12_done, w12_ready = sem("h_w12_done"), sem("h_w12_ready")
        xt_done, xt_ready = sem("h_xt_done"), sem("h_xt_ready")
        qk_done, q_high, k_high, qk_taken = sem("h_qk_done"), sem("h_q_high"), sem("h_k_high"), sem("h_qk_taken")

        block = c.enter_context(nc.Block())

        @block.sync
        def _(sp):
            sp.dma_start(xs[:], x).then_inc(loaded, 16)
            sp.dma_start(ident[:], ident_in).then_inc(loaded, 16)
            sp.dma_start(w1t[:], W1T).then_inc(loaded, 16)
            sp.dma_start(w2[:], W2).then_inc(loaded, 16)
            for half in range(2):
                sp.dma_start(wk2[:, :, half * DA:(half + 1) * DA],
                             W3.rearrange("(c p) n -> p c n", p=P)).then_inc(loaded, 16)
            with sp.Fori(0, NPAIR) as m:
                for u in range(2):
                    sp.wait_ge(h_ready, 2 * m + u + 1)
                    sp.dma_start(h_d[bass.ds(2 * m + u, 1)].rearrange("a p d -> p (a d)"), hrow[:, u, :]).then_inc(h_stored, 16)
            sp.wait_ge(h_stored, 16 + 16 * NT)

        @block.vector
        def _(dve):
            own = Own(dve, own_dve)
            dve.wait_ge(loaded, 96)
            nc.vector.tensor_copy(identh[:], ident[:]).then_inc(consts, 1)
            nc.vector.memset(hb[:, :, D:D + 2], 1.0).then_inc(consts, 1)
            env["normalize"](own, var_ready, root_ready, xs, sq, mean, var, root, inv, tmp)
            base = own.n
            PER = 3
            dve.sem_inc(h_stored, 16)
            dve.sem_inc(xt_done, 1)
            with dve.Fori(0, NPAIR) as m:
                for u in range(2):
                    t = 2 * m + u
                    own.start(base + PER * t)
                    row = hrow[:, u, :]
                    dve.wait_ge(h_stored, 16 + 32 * m)
                    dve.wait_ge(xt_done, 1 + 2 * m)
                    ins = nc.vector.tensor_scalar(row, flat(xs[:, bass.ds(t, 1), :]), 0.0, None, ALU.max)
                    ins.then_inc(h_ready, 1)
                    dve.wait_ge(h_ready, t + 1)
                    own.link(nc.vector.tensor_copy(hb[:, bass.ds(t, 1), 0:D].rearrange("p a d -> p (a d)"), row))
                    own.link(nc.vector.tensor_tensor(hb[:, bass.ds(t, 1), D + 2:HROW].rearrange("p a d -> p (a d)"), row,
                                                     hb[:, bass.ds(t, 1), 0:D].rearrange("p a d -> p (a d)"), ALU.subtract))
                    cols = bass.ds(t * P, P)
                    dve.wait_ge(k_high, t + 1)
                    nc.vector.tensor_tensor(kl2[:, cols], psum[2][:, 0:P], kh2[:, cols], ALU.subtract)
                    dve.wait_ge(q_high, t + 1)
                    own.link(nc.vector.tensor_tensor(qs[DA:P, cols], psum[3][DA:P, 0:P], q16[DA:P, 0, :], ALU.subtract))
                    nc.vector.tensor_copy(qs[0:DA, cols], q16[0:DA, 0, :]).then_inc(qk_taken, 1)

        @block.scalar
        def _(act):
            act.wait_ge(w12_done, 1)
            for half in range(2):
                nc.scalar.activation(wq2[:, :, half * DA:(half + 1) * DA],
                                     psum[0][:, 0:KC * DA].rearrange("p (c n) -> p c n", c=KC), ACT.Copy).then_inc(w12_ready, 1)
            env["square_and_root"](act, var_ready, root_ready, xs, sq, var, root)
            act.sem_inc(qk_taken, 1)
            with act.Fori(0, NPAIR) as m:
                for u in range(2):
                    t = 2 * m + u
                    act.wait_ge(xt_done, 1 + t + 1)
                    nc.scalar.activation(xT[:, u], psum[1][:, 0:D].rearrange("p (c n) -> p c n", c=KC), ACT.Copy).then_inc(xt_ready, 1)
                    act.wait_ge(qk_done, t + 1)
                    nc.scalar.activation(kh2[:, bass.ds(t * P, P)], psum[2][:, 0:P], ACT.Copy).then_inc(k_high, 1)
                    act.wait_ge(qk_taken, 1 + t)
                    nc.scalar.activation(q16[:, 0, :], psum[3][:, 0:P], ACT.Copy).then_inc(q_high, 1)

        @block.tensor
        def _(pe):
            pe.wait_ge(loaded, 96)
            for k in range(KC):
                last = nc.tensor.matmul(psum[0][:, k * DA:(k + 1) * DA], w1t[:, k * P:(k + 1) * P], w2[:], start=True, stop=True)
            last.then_inc(w12_done, 1)
            pe.wait_ge(w12_ready, 2)
            pe.sem_inc(xt_ready, 1)
            with pe.Fori(0, NPAIR) as m:
                for u in range(2):
                    t = 2 * m + u
                    pe.wait_ge(h_ready, t + 1)
                    pe.wait_ge(xt_ready, 1 + t)
                    for k in range(KC):
                        last = nc.tensor.transpose(psum[1][:, k * P:(k + 1) * P], hrow[:, u, k * P:(k + 1) * P], ident[:])
                    last.then_inc(xt_done, 1)
                    pe.wait_ge(xt_ready, 1 + t + 1)
                    pe.wait_ge(qk_taken, 1 + t)
                    for w, bank in ((wk2, 2), (wq2, 3)):
                        for k in range(KC):
                            last = nc.tensor.matmul(psum[bank][:, 0:P], w[:, k, :], xT[:, u, k, :], start=(k == 0), stop=(k == KC - 1))
                    last.then_inc(qk_done, 1)


def layer_step(nc, sem, psL, psT, psA, psS, sb_in, s, qs, kh2, kl2, adjT, identh, ident,
               a_high, a_low, s_high, s_low, sx_d, xa_d, rsum, csum):
    SW = D * (s + 1)
    tag = f"s{s}_"
    with ExitStack() as c:
        sb = sb_in(c)
        rows = sb(tag + "rows", [P, 4, NPAD], F32)
        dump = sb(tag + "dump", [P, NPAD], BF16)
        slab = sb(tag + "slab", [P, 2, HALF, P], F32)
        sh = sb(tag + "sh", [P, 2, HALF, P], F16)
        sl = sb(tag + "sl", [P, 2, HALF, P], F16)
        wh = sb(tag + "wh", [P, 2, CH], F16)
        wl = sb(tag + "wl", [P, 2, CH], F16)
        sx_out = sb(tag + "sx_out", [P, 2, SW], F32)
        xa_out = sb(tag + "xa_out", [P, 2, D], F32)
        mx = sb(tag + "mx", [P, 2, 2, NCH], F32)
        nb = sb(tag + "nb", [P, 2, 2], F32)
        Z = sb(tag + "Z", [P, 2, 2], F32)
        target, low, mid, mass, above, kept, rk = (
            sb(tag + n, [P, 2], F32) for n in ("target", "low", "mid", "mass", "above", "kept", "rk"))
        if s == 0:
            colacc = sb("colacc", [P, NT, P], F32)

        S = {n: sem(tag + n) for n in (
            "lg_done", "lg_free", "nb_ready", "exp_done", "w_ready", "rk_ready", "tr_done", "hi_done", "lo_done",
            "ax_done", "acc_free", "xa_stored", "slab_in0", "slab_in1", "sh_done", "sl_done", "half_used",
            "sa_free", "sx_stored", "own_dve", "own_pool", "rows_zero")}

        def pairs(eng, body):
            with eng.Fori(0, (NPAIR - 1) // 2) as m:
                body(2 * m, 0, False)
                body(2 * m + 1, 1, False)
            body(NPAIR - 1, 0, True)

        block = c.enter_context(nc.Block())

        @block.sync
        def _(sp):
            with sp.Fori(0, NT) as t:
                for f in range(2):
                    sp.wait_ge(S["sl_done"], 2 * t + f + 1)
                    if s == 0:
                        sp.wait_ge(S["own_pool"], 2 * t + f + 1)
                    sp.dma_start(slab[:, f], adjT[bass.ds(t, 1), :, f * HALF:(f + 1) * HALF, :].rearrange(
                        "a p j i -> p (a j) i")).then_inc(S[f"slab_in{f}"], 16)

        @block.gpsimd
        def _(pool):
            own = Own(pool, S["own_pool"])
            if s == 0:
                nc.gpsimd.memset(colacc[:], 0.0).then_inc(S["own_pool"], 2)
            with pool.Fori(0, NT) as t:
                for f in range(2):
                    h = 2 * t + f
                    pool.wait_ge(S["sh_done"], h + 1)
                    pool.wait_ge(S["half_used"], h + 1)
                    if s == 0:
                        pool.wait_ge(S["own_pool"], 2 + h)
                        nc.gpsimd.tensor_tensor(colacc[:, f * HALF:(f + 1) * HALF, :], colacc[:, f * HALF:(f + 1) * HALF, :],
                                                slab[:, f], ALU.add).then_inc(S["own_pool"], 1)
                    nc.gpsimd.tensor_tensor(sl[:, f], slab[:, f], sh[:, f], ALU.subtract).then_inc(S["sl_done"], 1)

        @block.scalar
        def _(act):
            act.wait_ge(S["rows_zero"], 1)

            def exps(kk, par):
                act.wait_ge(S["nb_ready"], kk + 1)
                for u in range(2):
                    r = rows[:, 2 * par + u, 0:N]
                    nc.scalar.activation(r, r, ACT.Exp, bias=nb[:, par, u:u + 1],
                                         accum_out=Z[:, par, u:u + 1]).then_inc(S["exp_done"], 1)

            def body(k, par, last):
                if not last:
                    exps(k + 1, 1 - par)
                for u in range(2):
                    for f in range(2):
                        h = 4 * k + 2 * u + f
                        act.wait_ge(S[f"slab_in{f}"], 16 * (2 * k + u + 1))
                        act.wait_ge(S["half_used"], h + 1)
                        nc.scalar.activation(sh[:, f], slab[:, f], ACT.Copy).then_inc(S["sh_done"], 1)
                    t = 2 * k + u
                    act.wait_ge(S["half_used"], 2 + 2 * (t + 1))
                    act.wait_ge(S["sx_stored"], 16 + 16 * t)
                    if s == 0:
                        nc.scalar.activation(rsum[:, bass.ds(t, 1)], psS[u][:, D:D + 1], ACT.Copy)
                    nc.scalar.activation(sx_out[:, u], psS[u][:, 0:SW], ACT.Copy).then_inc(S["sa_free"], 1)
                    act.wait_ge(S["sa_free"], 2 + t + 1)
                    act.dma_start(sx_d[bass.ds(t, 1)].rearrange("a p d -> p (a d)"), sx_out[:, u]).then_inc(S["sx_stored"], 16)
                for u in range(2):
                    for q in range(NGRP):
                        g = NGRP * u + q
                        w = P * len(group_blocks(q))
                        act.wait_ge(S["tr_done"], 2 * NGRP * k + g + 1)
                        act.wait_ge(S["ax_done"], 2 * NGRP * k + g + 1)
                        nc.scalar.activation(wh[:, g % 2, 0:w], psT[g % 2][:, 0:w], ACT.Copy).then_inc(S["hi_done"], 1)
                    t = 2 * k + u
                    act.wait_ge(S["ax_done"], 2 + NGRP * (t + 1))
                    act.wait_ge(S["rk_ready"], k + 1)
                    act.wait_ge(S["xa_stored"], 16 + 16 * t)
                    nc.scalar.activation(xa_out[:, u], psA[u][:, 0:D], ACT.Copy, scale=rk[:, u:u + 1]).then_inc(S["acc_free"], 1)
                    act.wait_ge(S["acc_free"], 2 + t + 1)
                    act.dma_start(xa_d[bass.ds(t, 1)].rearrange("a p d -> p (a d)"), xa_out[:, u]).then_inc(S["xa_stored"], 16)

            act.sem_inc(S["sx_stored"], 16)
            act.sem_inc(S["xa_stored"], 16)
            exps(0, 0)
            pairs(act, body)
            act.wait_ge(S["sx_stored"], 16 + 16 * NT)
            act.wait_ge(S["xa_stored"], 16 + 16 * NT)

        @block.vector
        def _(dve):
            own = Own(dve, S["own_dve"])
            nc.vector.memset(rows[:, :, N:NPAD], 0.0).then_inc(S["rows_zero"], 1)

            def take_logits(kk, par):
                for u in range(2):
                    for ch in range(NCH):
                        g = NCH * u + ch
                        w = chunk_width(ch)
                        dve.wait_ge(S["lg_done"], 2 * NCH * kk + g + 1)
                        nc.vector.tensor_scalar(rows[:, 2 * par + u, ch * CH:ch * CH + w], psL[g % 2][:, 0:w], 1.0, None,
                                                ALU.mult, ALU.max, accum_out=mx[:, par, u, ch:ch + 1]).then_inc(S["lg_free"], 1)
                dve.wait_ge(S["lg_free"], 2 + 2 * NCH * (kk + 1))
                own.link(nc.vector.tensor_reduce(nb[:, par], mx[:, par], AX.X, ALU.max, negate=True))
                nc.vector.tensor_scalar(nb[:, par], nb[:, par], LN_PSCALE, None, ALU.add).then_inc(S["nb_ready"], 1)

            def body(k, par, last):
                own.start(FIRST + PER * k)
                if not last:
                    take_logits(k + 1, 1 - par)
                dve.wait_ge(S["exp_done"], 2 * (k + 1))
                own.link(nc.vector.tensor_scalar(target[:], Z[:, par], P_NUC, None, ALU.mult))
                own.link(nc.vector.tensor_scalar(low[:], Z[:, par], LEAST, None, ALU.mult))
                for it in range(BISECT):
                    own.link(nc.vector.tensor_scalar(mid[:], low[:], 2.0 ** (LOG_STEP / 2 ** it), None, ALU.mult))
                    for u in range(2):
                        r = rows[:, 2 * par + u, 0:N]
                        own.link(nc.vector.scalar_tensor_tensor(out=dump[:, 0:N], in0=r, scalar=mid[:, u:u + 1], in1=r,
                                                                op0=ALU.is_gt, op1=ALU.mult, accum_out=mass[:, u:u + 1]))
                    own.link(nc.vector.tensor_tensor(above[:], mass[:], target[:], ALU.is_ge))
                    own.link(nc.vector.tensor_tensor(above[:], above[:], mid[:], ALU.mult))
                    own.link(nc.vector.tensor_tensor(low[:], low[:], above[:], ALU.max))
                for u in range(2):
                    r = rows[:, 2 * par + u, 0:N]
                    nc.vector.scalar_tensor_tensor(out=r, in0=r, scalar=low[:, u:u + 1], in1=r,
                                                   op0=ALU.is_gt, op1=ALU.mult, accum_out=kept[:, u:u + 1]).then_inc(S["w_ready"], 1)
                dve.wait_ge(S["w_ready"], 2 * (k + 1))
                dve.wait_ge(S["acc_free"], 2 + 2 * k)
                nc.vector.reciprocal(rk[:], kept[:]).then_inc(S["rk_ready"], 1)
                for g in range(2 * NGRP):
                    w = P * len(group_blocks(g % NGRP))
                    dve.wait_ge(S["hi_done"], 2 * NGRP * k + g + 1)
                    nc.vector.tensor_tensor(wl[:, g % 2, 0:w], psT[g % 2][:, 0:w], wh[:, g % 2, 0:w],
                                            ALU.subtract).then_inc(S["lo_done"], 1)
                if not last:
                    assert own.n == PER, own.n

            FIRST, PER = 1, 1 + 2 + 6 * BISECT
            own.start(0)
            take_logits(0, 0)
            pairs(dve, body)

            if s == 0:
                dve.wait_ge(S["own_pool"], 1 + 2 * NT)
                own.start(FIRST + PER * (NPAIR - 1) + own.n)
                own.link(nc.vector.tensor_reduce(csum[:], colacc[:], AX.X, ALU.add))

        @block.tensor
        def _(pe):
            pe.wait_ge(S["rows_zero"], 1)

            def logits(kk):
                for u in range(2):
                    t = 2 * kk + u
                    for ch in range(NCH):
                        g = NCH * u + ch
                        w = chunk_width(ch)
                        pe.wait_ge(S["lg_free"], 2 * NCH * kk + g + 1)
                        cols = slice(ch * CH, ch * CH + w)
                        lhs = qs[:, t * P:(t + 1) * P] if isinstance(t, int) else qs[:, bass.ds(t * P, P)]
                        nc.tensor.matmul(psL[g % 2][:, 0:w], lhs, kh2[:, cols], start=True, stop=False)
                        nc.tensor.matmul(psL[g % 2][:, 0:w], lhs, kl2[:, cols], start=False, stop=True).then_inc(S["lg_done"], 1)

            def sweep(k):
                for u in range(2):
                    t = 2 * k + u
                    acc = psS[u]
                    pe.wait_ge(S["sa_free"], t + 1)
                    tt = bass.ds(t, 1)

                    def own_row(part):
                        ap = part(tt)
                        return ap.rearrange("p a d -> p (a d)")
                    nh = SW + (1 - s)
                    nc.tensor.matmul(acc[:, 0:nh], identh[:], own_row(s_high), start=True, stop=False)
                    nc.tensor.matmul(acc[:, 0:SW], identh[:], own_row(s_low), start=False, stop=False, skip_group_check=True)
                    for f in range(2):
                        h = 4 * k + 2 * u + f
                        pe.wait_ge(S["sh_done"], h + 1)
                        pe.wait_ge(S["sl_done"], 2 + h + 1)
                        for jj in range(HALF):
                            j = f * HALF + jj
                            nc.tensor.matmul(acc[:, 0:nh], sh[:, f, jj, :], s_high(j), start=False, stop=False)
                            nc.tensor.matmul(acc[:, 0:SW], sh[:, f, jj, :], s_low(j), start=False, stop=False, skip_group_check=True)
                            ins = nc.tensor.matmul(acc[:, 0:nh], sl[:, f, jj, :], s_high(j), start=False, stop=(j == NT - 1))
                        ins.then_inc(S["half_used"], 1)

            def transposes(k, par, g):
                u, q = divmod(g, NGRP)
                pe.wait_ge(S["lo_done"], 2 * NGRP * k + g + 1)
                for n, j in enumerate(group_blocks(q)):
                    ins = nc.tensor.transpose(psT[g % 2][:, n * P:(n + 1) * P], rows[:, 2 * par + u, j * P:(j + 1) * P], ident[:])
                ins.then_inc(S["tr_done"], 1)

            def attend(k, g):
                u, q = divmod(g, NGRP)
                acc = psA[u][:, 0:D]
                if q == 0:
                    pe.wait_ge(S["acc_free"], 2 * k + u + 1)
                pe.wait_ge(S["lo_done"], 2 + 2 * NGRP * k + g + 1)
                for n, j in enumerate(group_blocks(q)):
                    blk = slice(n * P, (n + 1) * P)
                    nc.tensor.matmul(acc, wh[:, g % 2, blk], a_high(j), start=(j == 0), stop=False)
                    nc.tensor.matmul(acc, wh[:, g % 2, blk], a_low(j), start=False, stop=False)
                    ins = nc.tensor.matmul(acc, wl[:, g % 2, blk], a_high(j), start=False, stop=(j == NT - 1))
                ins.then_inc(S["ax_done"], 1)

            def body(k, par, last):
                if not last:
                    logits(k + 1)
                sweep(k)
                for g in range(2 * NGRP + 1):
                    if g < 2 * NGRP:
                        if g % NGRP == 0:
                            pe.wait_ge(S["w_ready"], 2 * k + g // NGRP + 1)
                        transposes(k, par, g)
                    if g >= 1:
                        attend(k, g - 1)

            for n in ("lg_free", "ax_done", "lo_done", "acc_free", "half_used", "sa_free", "sl_done"):
                pe.sem_inc(S[n], 2)
            logits(0)
            pairs(pe, body)


def phase_between(nc, sem, psum, sb_in, env):
    U1, U2, U3 = env["U1"], env["U2"], env["U3"]
    ident, x2h, x2l, xab, h_d, z_d = (env[n] for n in ("ident", "x2h", "x2l", "xab", "h_d", "z_d"))
    sx_d, xa_d, rinv, cinv, rsum, csum = (env[n] for n in ("sx_d", "xa_d", "rinv", "cinv", "rsum", "csum"))
    qs, kh2, kl2, wq2, wk2 = (env[n] for n in ("qs", "kh2", "kl2", "wq2", "wk2"))
    with ExitStack() as c:
        sb = sb_in(c)
        u12 = sb("b_u12", [P, KC, 2 * D], F32)
        u3 = sb("b_u3", [P, KC, D], F32)
        tin = sb("b_tin", [P, 2, 3, D], F32)
        x2 = sb("b_x2", [P, 2, D], F32)
        xT = sb("b_xT", [P, 2, 2 * KC, P], F32)
        q16 = sb("b_q16", [P, P], F16)
        z = sb("b_z", [P, 2, D], F32)
        loaded, own_dve, own_sp = sem("b_loaded"), sem("b_own_dve"), sem("b_scales")
        t_in = [sem("b_tin0"), sem("b_tin1")]
        xt_done, xt_ready = sem("b_xt_done"), sem("b_xt_ready")
        qk_done, q_high, k_high, uz_done, z_ready, z_stored = (sem("b_" + n) for n in (
            "qk_done", "q_high", "k_high", "uz_done", "z_ready", "z_stored"))
        block = c.enter_context(nc.Block())

        @block.sync
        def _(sp):
            sp.dma_start(u12[:, :, 0:D], U1[0].rearrange("(c p) n -> p c n", p=P)).then_inc(loaded, 16)
            sp.dma_start(u12[:, :, D:2 * D], U2[0].rearrange("(c p) n -> p c n", p=P)).then_inc(loaded, 16)
            sp.dma_start(u3[:], U3[0].rearrange("(c p) n -> p c n", p=P)).then_inc(loaded, 16)
            with sp.Fori(0, NPAIR) as m:
                for u in range(2):
                    t = 2 * m + u
                    sp.wait_ge(z_ready, 1 + 2 * m)
                    for n, dram in enumerate((sx_d[0], xa_d[0], h_d)):
                        sp.dma_start(tin[:, u, n, :], dram[bass.ds(t, 1)].rearrange("a p d -> p (a d)")).then_inc(t_in[u], 16)

        @block.vector
        def _(dve):
            own = Own(dve, own_dve)
            own.link(nc.vector.tensor_scalar(csum[:], csum[:], 1.0, None, ALU.add))
            own.link(nc.vector.tensor_scalar(csum[:], csum[:], 1e-12, None, ALU.max))
            own.link(nc.vector.reciprocal(cinv[:], csum[:]))
            own.link(nc.vector.tensor_scalar(rsum[:], rsum[:], 1e-12, None, ALU.max))
            own.link(nc.vector.reciprocal(rinv[:], rsum[:]))
            PER = 8
            with dve.Fori(0, NPAIR) as m:
                for u in range(2):
                    t = 2 * m + u
                    own.start(5 + PER * t)
                    t1 = bass.ds(t, 1)
                    cols = bass.ds(t * P, P)
                    dve.wait_ge(t_in[u], 48 * (m + 1))
                    own.link(nc.vector.tensor_scalar(x2[:, 0], tin[:, u, 0], rinv[:, t1], None, ALU.mult))
                    own.link(nc.vector.tensor_scalar(x2[:, 1], tin[:, u, 0], cinv[:, t1], None, ALU.mult))
                    x2f = x2[:].rearrange("p a d -> p (a d)")
                    own.link(nc.vector.tensor_copy(flat(x2h[:, t1, :]), x2f))
                    own.link(nc.vector.tensor_tensor(flat(x2l[:, t1, :]), x2f, flat(x2h[:, t1, :]), ALU.subtract))
                    own.link(nc.vector.tensor_copy(flat(xab[:, t1, 0:D]), tin[:, u, 1]))
                    own.link(nc.vector.tensor_tensor(flat(xab[:, t1, D:2 * D]), tin[:, u, 1], flat(xab[:, t1, 0:D]), ALU.subtract))
                    dve.wait_ge(k_high, t + 1)
                    nc.vector.tensor_tensor(kl2[:, cols], psum[2][:, 0:P], kh2[:, cols], ALU.subtract)
                    dve.wait_ge(q_high, t + 1)
                    nc.vector.tensor_tensor(qs[DA:P, cols], psum[3][DA:P, 0:P], q16[DA:P, :], ALU.subtract)
                    nc.vector.tensor_copy(qs[0:DA, cols], q16[0:DA, :])
                    dve.wait_ge(uz_done, t + 1)
                    dve.wait_ge(z_stored, 16 + 16 * t)
                    own.link(nc.vector.tensor_tensor(z[:, u], psum[5][:, 0:D], tin[:, u, 2], ALU.add))
                    own.link(nc.vector.scalar_tensor_tensor(out=z[:, u], in0=psum[4][:, 0:D], scalar=rinv[:, t1], in1=z[:, u],
                                                            op0=ALU.mult, op1=ALU.add))
                    nc.vector.scalar_tensor_tensor(out=z[:, u], in0=psum[4][:, D:2 * D], scalar=cinv[:, t1], in1=z[:, u],
                                                   op0=ALU.mult, op1=ALU.add).then_inc(z_ready, 1)
                    dve.wait_ge(z_ready, 1 + t + 1)

        @block.scalar
        def _(act):
            with act.Fori(0, NPAIR) as m:
                for u in range(2):
                    t = 2 * m + u
                    act.wait_ge(xt_done, t + 1)
                    nc.scalar.activation(xT[:, u], psum[1][:].rearrange("p (c n) -> p c n", n=P), ACT.Copy).then_inc(xt_ready, 1)
                    act.wait_ge(qk_done, t + 1)
                    nc.scalar.activation(kh2[:, bass.ds(t * P, P)], psum[2][:, 0:P], ACT.Copy).then_inc(k_high, 1)
                    act.wait_ge(z_ready, 1 + t)
                    nc.scalar.activation(q16[:], psum[3][:, 0:P], ACT.Copy).then_inc(q_high, 1)
                    act.wait_ge(z_ready, 1 + t + 1)
                    act.dma_start(z_d[bass.ds(t, 1)].rearrange("a p d -> p (a d)"), z[:, u]).then_inc(z_stored, 16)
            act.wait_ge(z_stored, 16 + 16 * NT)

        @block.tensor
        def _(pe):
            pe.wait_ge(loaded, 48)
            pe.sem_inc(xt_ready, 1)
            pe.sem_inc(z_ready, 1)
            pe.sem_inc(z_stored, 16)
            with pe.Fori(0, NPAIR) as m:
                for u in range(2):
                    t = 2 * m + u
                    pe.wait_ge(t_in[u], 48 * (m + 1))
                    pe.wait_ge(xt_ready, 1 + t)
                    for n in range(2):
                        for k in range(KC):
                            b = n * KC + k
                            last = nc.tensor.transpose(psum[1][:, b * P:(b + 1) * P], tin[:, u, n, k * P:(k + 1) * P], ident[:])
                    last.then_inc(xt_done, 1)
                    pe.wait_ge(xt_ready, 1 + t + 1)
                    pe.wait_ge(z_ready, 1 + t)
                    for w, bank in ((wk2, 2), (wq2, 3)):
                        for k in range(KC):
                            last = nc.tensor.matmul(psum[bank][:, 0:P], w[:, k, :], xT[:, u, KC + k, :], start=(k == 0), stop=(k == KC - 1))
                    last.then_inc(qk_done, 1)
                    for k in range(KC):
                        nc.tensor.matmul(psum[4][:], xT[:, u, k, :], u12[:, k, :], start=(k == 0), stop=(k == KC - 1))
                    for k in range(KC):
                        last = nc.tensor.matmul(psum[5][:, 0:D], xT[:, u, KC + k, :], u3[:, k, :], start=(k == 0), stop=(k == KC - 1))
                    last.then_inc(uz_done, 1)


def flat(ap):
    return ap.rearrange("p a d -> p (a d)")


def phase_mid(nc, sem, psum, sb_in, env):
    U1, U2, U3 = env["U1"], env["U2"], env["U3"]
    ident, z_d, x1_d = env["ident"], env["z_d"], env["x1_d"]
    sx_d, xa_d, rinv, cinv = (env[n] for n in ("sx_d", "xa_d", "rinv", "cinv"))
    hth, htl, sup, natt = (env[n] for n in ("hth", "htl", "sup", "natt"))
    with ExitStack() as c:
        sb = sb_in(c)
        u12 = sb("m_u12", [P, KC, 2 * D], F32)
        u3 = sb("m_u3", [P, KC, D], F32)
        wt = sb("m_wt", [P, KC, D], F32)
        ew = sb("m_ew", [P, KC, D], F32)
        nw = sb("m_nw", [P, KC, 1], F32)
        gam = sb("m_gam", [P, D], F32)
        bet = sb("m_bet", [P, D], F32)
        y = sb("m_y", [P, NT, D], F32)
        sq = sb("m_sq", [P, NT, D], F32)
        xx = sb("m_x", [P, NT, D], F32)
        tin = sb("m_tin", [P, 2, 4, D], F32)
        xT = sb("m_xT", [P, 6, P], F32)
        h2 = sb("m_h2", [P, D], F32)
        hT = sb("m_hT", [P, KC, P], F32)
        mean, var, root, inv, tmp = (sb("m_" + n, [P, NT], F32) for n in ("mean", "var", "root", "inv", "tmp"))
        col = sb("m_col", [P, 4], F32)
        natt_in = sb("m_natt", [P, NT], F32)
        loaded, own_dve = sem("m_loaded"), sem("m_own_dve")
        t_in = [sem("m_tin0"), sem("m_tin1")]
        xt_done, xt_ready, uz_done, y_ready = (sem("m_" + n) for n in ("xt_done", "xt_ready", "uz_done", "y_ready"))
        var_ready = [sem("m_var0"), sem("m_var1")]
        root_ready = [sem("m_root0"), sem("m_root1")]
        x1_ready, x1_stored = sem("m_x1_ready"), sem("m_x1_stored")
        h2_ready, ht_done, ht_ready, pr_done, hi_ready, pr_taken = (sem("m_" + n) for n in (
            "h2_ready", "ht_done", "ht_ready", "pr_done", "hi_ready", "pr_taken"))
        na = [sem(f"m_na{i}") for i in range(6)]
        block = c.enter_context(nc.Block())

        @block.sync
        def _(sp):
            def w2d(ap):
                return ap.rearrange("(c p) n -> p c n", p=P)
            sp.dma_start(u12[:, :, 0:D], w2d(U1[1])).then_inc(loaded, 16)
            sp.dma_start(u12[:, :, D:2 * D], w2d(U2[1])).then_inc(loaded, 16)
            sp.dma_start(u3[:], w2d(U3[1])).then_inc(loaded, 16)
            sp.dma_start(wt[:], w2d(env["weight"])).then_inc(loaded, 16)
            sp.dma_start(ew[:], w2d(env["edge_w"])).then_inc(loaded, 16)
            sp.dma_start(nw[:, :, 0], env["node_w"]).then_inc(loaded, 16)
            sp.dma_start(gam[:], env["gamma"]).then_inc(loaded, 16)
            sp.dma_start(bet[:], env["beta"]).then_inc(loaded, 16)
            sp.dma_start(xx[:], env["x"]).then_inc(loaded, 16)
            with sp.Fori(0, NPAIR) as m:
                for u in range(2):
                    t = 2 * m + u
                    sp.wait_ge(y_ready, 1 + 2 * m)
                    sp.dma_start(tin[:, u, 0:2, :].rearrange("p a d -> p (a d)"), flat(sx_d[1][bass.ds(t, 1)].rearrange("a p d -> p a d"))).then_inc(t_in[u], 16)
                    for n, dram in ((2, xa_d[1]), (3, z_d)):
                        sp.dma_start(tin[:, u, n, :], flat(dram[bass.ds(t, 1)].rearrange("a p d -> p a d"))).then_inc(t_in[u], 16)
            sp.wait_ge(x1_ready, 1)
            sp.dma_start(x1_d, xx[:]).then_inc(x1_stored, 16)
            sp.wait_ge(x1_stored, 16)

        @block.vector
        def _(dve):
            own = Own(dve, own_dve)
            dve.wait_ge(loaded, 144)
            with dve.Fori(0, NPAIR) as m:
                for u in range(2):
                    t = 2 * m + u
                    t1 = bass.ds(t, 1)
                    own.start(2 * t)
                    yt = flat(y[:, t1, :])
                    dve.wait_ge(t_in[u], 48 * (m + 1))
                    dve.wait_ge(uz_done, t + 1)
                    own.link(nc.vector.tensor_tensor(yt, psum[5][:, 0:D], tin[:, u, 3], ALU.add))
                    own.link(nc.vector.scalar_tensor_tensor(out=yt, in0=psum[4][:, 0:D], scalar=rinv[:, t1], in1=yt,
                                                            op0=ALU.mult, op1=ALU.add))
                    nc.vector.scalar_tensor_tensor(out=yt, in0=psum[4][:, D:2 * D], scalar=cinv[:, t1], in1=yt,
                                                   op0=ALU.mult, op1=ALU.add).then_inc(y_ready, 1)
            dve.wait_ge(y_ready, 1 + NT)
            own.start(2 * NT)
            env["normalize"](own, var_ready[0], root_ready[0], y, sq, mean, var, root, inv, tmp)
            wide = [P, NT, D]
            own.link(nc.vector.tensor_tensor(y[:], y[:], gam[:].unsqueeze(1).to_broadcast(wide), ALU.mult))
            own.link(nc.vector.tensor_tensor(y[:], y[:], bet[:].unsqueeze(1).to_broadcast(wide), ALU.add))
            nc.vector.tensor_tensor(xx[:], xx[:], y[:], ALU.add).then_inc(x1_ready, 1)
            dve.wait_ge(x1_ready, 1)
            own.link(nc.vector.tensor_copy(y[:], xx[:]))
            env["normalize"](own, var_ready[1], root_ready[1], y, sq, mean, var, root, inv, tmp)
            base = 2 * NT + own.n
            dve.sem_inc(ht_done, 1)
            with dve.Fori(0, NT) as t:
                t1 = bass.ds(t, 1)
                cols = bass.ds(t * P, P)
                dve.wait_ge(ht_done, 1 + t)
                nc.vector.tensor_scalar(h2[:], flat(y[:, t1, :]), 0.0, None, ALU.max).then_inc(h2_ready, 1)
                dve.wait_ge(hi_ready, 2 * (t + 1))
                nc.vector.tensor_tensor(htl[:, :, cols], psum[2][:, 0:D].rearrange("p (c n) -> p c n", c=KC), hth[:, :, cols], ALU.subtract)
                nc.vector.tensor_tensor(flat(sup[:, t1, D:2 * D]), psum[3][:, 0:D], flat(sup[:, t1, 0:D]), ALU.subtract)
                nc.vector.tensor_copy(natt_in[:, t1], psum[5][:, 0:1]).then_inc(pr_taken, 1)
            own.start(base)
            dve.wait_ge(na[0], 1)
            nc.vector.tensor_reduce(col[:, 0:1], natt[:], AX.X, ALU.max).then_inc(na[1], 1)
            dve.wait_ge(na[2], 1)
            nc.vector.tensor_scalar(col[:, 1:2], col[:, 1:2], -1.0, None, ALU.mult).then_inc(na[3], 1)
            dve.wait_ge(na[5], 1)
            own.link(nc.vector.reciprocal(col[:, 2:3], col[:, 3:4]))
            own.link(nc.vector.tensor_scalar(natt[:], natt[:], col[:, 2:3], None, ALU.mult))

        @block.gpsimd
        def _(pool):
            pool.wait_ge(pr_taken, 1 + NT)
            nc.gpsimd.affine_select(out=natt[:], in_=natt_in[:], pattern=[[-P, NT]], base=N - 1, channel_multiplier=-1,
                                    compare_op=ALU.is_ge, fill=-3e38).then_inc(na[0], 1)
            pool.wait_ge(na[1], 1)
            nc.gpsimd.partition_all_reduce(col[:, 1:2], col[:, 0:1], P, bass.bass_isa.ReduceOp.max).then_inc(na[2], 1)
            pool.wait_ge(na[4], 1)
            nc.gpsimd.partition_all_reduce(col[:, 3:4], col[:, 2:3], P, bass.bass_isa.ReduceOp.add).then_inc(na[5], 1)

        @block.scalar
        def _(act):
            with act.Fori(0, NT) as t:
                act.wait_ge(xt_done, t + 1)
                act.wait_ge(y_ready, 1 + t)
                nc.scalar.activation(xT[:, 0:4], psum[0][:].rearrange("p (c n) -> p c n", n=P), ACT.Copy)
                nc.scalar.activation(xT[:, 4:6], psum[1][:, 0:D].rearrange("p (c n) -> p c n", n=P), ACT.Copy).then_inc(xt_ready, 1)
            for n in range(2):
                env["square_and_root"](act, var_ready[n], root_ready[n], y, sq, var, root)
            with act.Fori(0, NT) as t:
                cols = bass.ds(t * P, P)
                act.wait_ge(ht_done, 1 + t + 1)
                nc.scalar.activation(hT[:], psum[1][:, 0:D].rearrange("p (c n) -> p c n", n=P), ACT.Copy).then_inc(ht_ready, 1)
                act.wait_ge(pr_done, t + 1)
                nc.scalar.activation(hth[:, :, cols], psum[2][:, 0:D].rearrange("p (c n) -> p c n", c=KC), ACT.Copy).then_inc(hi_ready, 1)
                nc.scalar.activation(flat(sup[:, bass.ds(t, 1), 0:D]), psum[3][:, 0:D], ACT.Copy).then_inc(hi_ready, 1)
            act.wait_ge(na[3], 1)
            nc.scalar.activation(natt[:], natt[:], ACT.Exp, bias=col[:, 1:2], accum_out=col[:, 2:3]).then_inc(na[4], 1)

        @block.tensor
        def _(pe):
            pe.wait_ge(loaded, 144)
            for semaphore in (xt_ready, y_ready, ht_ready, pr_taken):
                pe.sem_inc(semaphore, 1)
            with pe.Fori(0, NPAIR) as m:
                for u in range(2):
                    t = 2 * m + u
                    pe.wait_ge(t_in[u], 48 * (m + 1))
                    pe.wait_ge(xt_ready, 1 + t)
                    for n in range(3):
                        for k in range(KC):
                            b = n * KC + k
                            last = nc.tensor.transpose(psum[b // 4][:, (b % 4) * P:(b % 4 + 1) * P], tin[:, u, n, k * P:(k + 1) * P], ident[:])
                    last.then_inc(xt_done, 1)
                    pe.wait_ge(xt_ready, 1 + t + 1)
                    pe.wait_ge(y_ready, 1 + t)
                    for n in range(2):
                        for k in range(KC):
                            nc.tensor.matmul(psum[4][:, n * D:(n + 1) * D], xT[:, n * KC + k, :], u12[:, k, n * D:(n + 1) * D],
                                             start=(k == 0), stop=(k == KC - 1))
                    for k in range(KC):
                        last = nc.tensor.matmul(psum[5][:, 0:D], xT[:, 2 * KC + k, :], u3[:, k, :], start=(k == 0), stop=(k == KC - 1))
                    last.then_inc(uz_done, 1)
            with pe.Fori(0, NT) as t:
                pe.wait_ge(h2_ready, t + 1)
                pe.wait_ge(ht_ready, 1 + t)
                for k in range(KC):
                    last = nc.tensor.transpose(psum[1][:, k * P:(k + 1) * P], h2[:, k * P:(k + 1) * P], ident[:])
                last.then_inc(ht_done, 1)
                pe.wait_ge(ht_ready, 1 + t + 1)
                pe.wait_ge(pr_taken, 1 + t)
                for d in range(KC):
                    for k in range(KC):
                        nc.tensor.matmul(psum[2][:, d * P:(d + 1) * P], ew[:, k, d * P:(d + 1) * P], hT[:, k, :], start=(k == 0), stop=(k == KC - 1))
                for k in range(KC):
                    nc.tensor.matmul(psum[3][:, 0:D], hT[:, k, :], wt[:, k, :], start=(k == 0), stop=(k == KC - 1))
                for k in range(KC):
                    last = nc.tensor.matmul(psum[5][:, 0:1], hT[:, k, :], nw[:, k, :], start=(k == 0), stop=(k == KC - 1))
                last.then_inc(pr_done, 1)


def phase_edges(nc, sem, psum, sb_in, env):
    ident, adjR, x1_d, out = env["ident"], env["adjR"], env["x1_d"], env["out"]
    hth, htl, sup, natt = (env[n] for n in ("hth", "htl", "sup", "natt"))
    psL, psT, psA = psum[0:2], psum[2:4], psum[4:6]
    with ExitStack() as c:
        sb = sb_in(c)
        em = sb("e_rows", [P, 2, NPAD], F32)
        adj = sb("e_adj", [P, 2, NPAD], F32)
        pen = sb("e_pen", [P, 2, NPAD], BF16)
        identb = sb("e_identb", [P, P], BF16)
        wh = sb("e_wh", [P, 2, CH], F16)
        wl = sb("e_wl", [P, 2, CH], F16)
        xr = sb("e_xr", [P, 2, D], F32)
        bias = sb("e_bias", [P, D], F32)
        o = sb("e_out", [P, 2, D], F32)
        mx = sb("e_mx", [P, 2, NCH], F32)
        nb, den, fac = (sb("e_" + n, [P, 2], F32) for n in ("nb", "den", "fac"))
        S = {n: sem("e_" + n) for n in (
            "bias_in", "adj_in0", "adj_in1", "xr_in0", "xr_in1", "lg_done", "lg_free", "nb_ready", "exp_done", "w_ready",
            "tr_done", "hi_done", "lo_done", "ax_done", "out_ready", "out_stored0", "out_stored1", "own_dve", "zero", "pen_ready")}

        def tiles(eng, body):
            with eng.Fori(0, (NT - 2) // 2) as m:
                body(2 * m, m, 0, False)
                body(2 * m + 1, m, 1, False)
            body(NT - 2, NT // 2 - 1, 0, False)
            body(NT - 1, NT // 2 - 1, 1, True)

        block = c.enter_context(nc.Block())

        @block.sync
        def _(sp):
            def load(t, u):
                sp.dma_start(adj[:, u], flat(adjR[bass.ds(t, 1)].rearrange("a p d -> p a d"))).then_inc(S[f"adj_in{u}"], 16)

            def load_x(t, u):
                sp.dma_start(xr[:, u], flat(x1_d[:, bass.ds(t, 1), :])).then_inc(S[f"xr_in{u}"], 16)

            def store(t, u):
                sp.dma_start(flat(out[:, bass.ds(t, 1), :]), o[:, u]).then_inc(S[f"out_stored{u}"], 16)

            sp.dma_start(bias[:], env["bias"]).then_inc(S["bias_in"], 16)
            for t in range(2):
                load(t, t)
                load_x(t, t)
            with sp.Fori(1, NT // 2) as m:
                for u in range(2):
                    t = 2 * m + u
                    sp.wait_ge(S["w_ready"], t - 1)
                    load(t, u)
                    sp.wait_ge(S["out_ready"], t + 1)
                    load_x(t, u)
                    store(t - 2, u)
            for t in range(NT - 2, NT):
                sp.wait_ge(S["out_ready"], 2 + t + 1)
                store(t, t % 2)
            for u in range(2):
                sp.wait_ge(S[f"out_stored{u}"], 16 + 16 * (NT // 2))

        @block.gpsimd
        def _(pool):
            with pool.Fori(0, NT // 2) as m:
                for u in range(2):
                    t = 2 * m + u
                    pool.wait_ge(S["adj_in%d" % u], 16 * (m + 1))
                    pool.wait_ge(S["exp_done"], t + 1)
                    nc.gpsimd.tensor_tensor(em[:, u], em[:, u], adj[:, u], ALU.mult).then_inc(S["w_ready"], 1)

        @block.scalar
        def _(act):
            def exps(t, par):
                act.wait_ge(S["nb_ready"], t + 1)
                act.wait_ge(S["out_ready"], t + 1)
                nc.scalar.activation(em[:, par, 0:N], em[:, par, 0:N], ACT.Exp, bias=nb[:, par:par + 1],
                                     accum_out=den[:, par:par + 1]).then_inc(S["exp_done"], 1)

            def body(t, m, par, last):
                if not last:
                    exps(t + 1, 1 - par)
                for q in range(NGRP):
                    g = NGRP * t + q
                    b = (NGRP * par + q) % 2
                    w = P * len(group_blocks(q))
                    act.wait_ge(S["tr_done"], g + 1)
                    act.wait_ge(S["ax_done"], g + 1)
                    nc.scalar.activation(wh[:, b, 0:w], psT[b][:, 0:w], ACT.Copy).then_inc(S["hi_done"], 1)

            act.wait_ge(S["zero"], 1)
            exps(0, 0)
            tiles(act, body)

        @block.vector
        def _(dve):
            own = Own(dve, S["own_dve"])
            nc.vector.memset(em[:, :, N:NPAD], 0.0).then_inc(S["zero"], 1)
            PER = 3

            def penalty(t, par, m):
                dve.wait_ge(S[f"adj_in{par}"], 16 * (m + 1))
                if not isinstance(t, int):
                    dve.wait_ge(S["lg_done"], NCH * (t - 1))
                nc.vector.tensor_scalar(pen[:, par, 0:N], adj[:, par, 0:N], 0.0, NEG_BIG, ALU.is_le, ALU.mult).then_inc(S["pen_ready"], 1)

            def take(t, par):
                for ch in range(NCH):
                    b = (NCH * par + ch) % 2
                    w = chunk_width(ch)
                    dve.wait_ge(S["lg_done"], NCH * t + ch + 1)
                    nc.vector.tensor_scalar(em[:, par, ch * CH:ch * CH + w], psL[b][:, 0:w], 1.0, None, ALU.mult, ALU.max,
                                            accum_out=mx[:, par, ch:ch + 1]).then_inc(S["lg_free"], 1)
                dve.wait_ge(S["lg_free"], 2 + NCH * (t + 1))
                nc.vector.tensor_reduce(nb[:, par:par + 1], mx[:, par], AX.X, ALU.max, negate=True).then_inc(S["nb_ready"], 1)

            def body(t, m, par, last):
                own.start(1 + PER * t)
                if not last:
                    take(t + 1, 1 - par)
                for q in range(NGRP):
                    b = (NGRP * par + q) % 2
                    w = P * len(group_blocks(q))
                    dve.wait_ge(S["hi_done"], NGRP * t + q + 1)
                    nc.vector.tensor_tensor(wl[:, b, 0:w], psT[b][:, 0:w], wh[:, b, 0:w], ALU.subtract).then_inc(S["lo_done"], 1)
                if not isinstance(t, int):
                    penalty(t + 2, par, m + 1)
                own.link(nc.vector.reciprocal(fac[:, par:par + 1], den[:, par:par + 1]))
                own.link(nc.vector.tensor_tensor(fac[:, par:par + 1], fac[:, par:par + 1], natt[:, bass.ds(t, 1)], ALU.mult))
                dve.wait_ge(S[f"xr_in{par}"], 16 * m + 16)
                own.link(nc.vector.tensor_tensor(xr[:, par], xr[:, par], bias[:], ALU.add))
                dve.wait_ge(S[f"out_stored{par}"], 16 + 16 * m)
                dve.wait_ge(S["ax_done"], 2 + NGRP * (t + 1))
                nc.vector.scalar_tensor_tensor(out=o[:, par], in0=psA[par][:, 0:D], scalar=fac[:, par:par + 1], in1=xr[:, par],
                                               op0=ALU.mult, op1=ALU.add).then_inc(S["out_ready"], 1)

            dve.wait_ge(S["bias_in"], 16)
            for u in range(2):
                dve.sem_inc(S[f"out_stored{u}"], 16)
            own.start(0)
            own.link(nc.vector.tensor_copy(identb[:], ident[:]))
            for u in range(2):
                penalty(u, u, 0)
            take(0, 0)
            tiles(dve, body)

        @block.tensor
        def _(pe):
            def scores(t, par):
                rows = bass.ds(t * P, P)
                pe.wait_ge(S["pen_ready"], t + 1)
                for ch in range(NCH):
                    b = (NCH * par + ch) % 2
                    w = chunk_width(ch)
                    cols = slice(ch * CH, ch * CH + w)
                    pe.wait_ge(S["lg_free"], NCH * t + ch + 1)
                    n = 0
                    for lhs, rhs in ((hth, hth), (hth, htl), (htl, hth)):
                        for k in range(KC):
                            ins = nc.tensor.matmul(psL[b][:, 0:w], lhs[:, k, rows], rhs[:, k, cols], start=(n == 0), stop=False)
                            n += 1
                    ins = nc.tensor.matmul(psL[b][:, 0:w], identb[:], pen[:, par, cols], start=False, stop=True)
                    ins.then_inc(S["lg_done"], 1)

            def body(t, m, par, last):
                if not last:
                    scores(t + 1, 1 - par)
                pe.wait_ge(S["w_ready"], t + 1)
                for q in range(NGRP + 1):
                    if q < NGRP:
                        b = (NGRP * par + q) % 2
                        pe.wait_ge(S["lo_done"], NGRP * t + q + 1)
                        for n, j in enumerate(group_blocks(q)):
                            ins = nc.tensor.transpose(psT[b][:, n * P:(n + 1) * P], em[:, par, j * P:(j + 1) * P], ident[:])
                        ins.then_inc(S["tr_done"], 1)
                    if q >= 1:
                        b = (NGRP * par + q - 1) % 2
                        if q == 1:
                            pe.wait_ge(S["out_ready"], t + 1)
                        pe.wait_ge(S["lo_done"], 2 + NGRP * t + q)
                        acc = psA[par][:, 0:D]
                        for n, j in enumerate(group_blocks(q - 1)):
                            blk = slice(n * P, (n + 1) * P)
                            nc.tensor.matmul(acc, wh[:, b, blk], sup[:, j, 0:D], start=(j == 0), stop=False)
                            nc.tensor.matmul(acc, wh[:, b, blk], sup[:, j, D:2 * D], start=False, stop=False)
                            ins = nc.tensor.matmul(acc, wl[:, b, blk], sup[:, j, 0:D], start=False, stop=(j == NT - 1))
                        ins.then_inc(S["ax_done"], 1)

            pe.wait_ge(S["zero"], 1)
            for n in ("lg_free", "ax_done", "lo_done", "out_ready"):
                pe.sem_inc(S[n], 2)
            scores(0, 0)
            tiles(pe, body)


_OUT = (P, NT, D)


def kernel(**inputs):
    import concourse.bacc as _bacc
    from concourse.bass_utils import run_bass_kernel_spmd as _run

    a = {k: np.asarray(v) for k, v in inputs.items()}
    x = np.zeros((NPAD, D), a["x"].dtype)
    x[:N] = a["x"]
    adj = np.zeros((NPAD, NPAD), a["adj"].dtype)
    adj[:N, :N] = a["adj"]

    def wide(v):
        return np.ascontiguousarray(np.broadcast_to(v[None, :], (P, v.shape[0])))

    arrays = {
        "x": np.ascontiguousarray(x.reshape(NT, P, D).transpose(1, 0, 2)),
        "adjT": np.ascontiguousarray(adj.reshape(NT, P, NT, P).transpose(0, 3, 2, 1)),
        "adjR": adj.reshape(NT, P, NPAD),
        "W1T": np.ascontiguousarray(a["L0_gnn_W1"].T),
        "W2": a["L0_gnn_W2"], "W3": a["L0_gnn_W3"],
        "U1": a["L0_gnn_U1"], "U2": a["L0_gnn_U2"], "U3": a["L0_gnn_U3"],
        "gamma": wide(a["L0_gnn_gamma"]), "beta": wide(a["L0_gnn_beta"]),
        "weight": a["L1_gnn_weight"], "bias": wide(a["L1_gnn_bias"]),
        "node_w": np.ascontiguousarray(a["L1_gnn_node_w"].reshape(KC, P).T), "edge_w": a["L1_gnn_edge_w"],
        "ident_in": np.eye(P, dtype=np.float32),
    }
    nc = _bacc.Bacc("TRN2", target_bir_lowering=False, num_devices=1)
    args = {k: nc.dram_tensor(k + "_dram", v.shape, mybir.dt.from_np(v.dtype), kind="ExternalInput").ap() for k, v in arrays.items()}
    out = nc.dram_tensor("out_dram", _OUT, F32, kind="ExternalOutput").ap()
    program(nc, out=out, **args)
    r = _run(nc, [{k + "_dram": v for k, v in arrays.items()}], core_ids=[0])
    got = r.results[0]["out_dram"]
    return np.ascontiguousarray(got.transpose(1, 0, 2)).reshape(NPAD, D)[:N]
```
